# Optimizing a Trainium2 kernel written in Bass

```python
import numpy as np
import jax
import jax.numpy as jnp

def _softmax(x, axis=-1):
    return jax.nn.softmax(x, axis=axis)

def _gelu(x):
    return jax.nn.gelu(x, approximate=True)

def _silu(x):
    return jax.nn.silu(x)

def _sigmoid(x):
    return jax.nn.sigmoid(x)

def _layernorm(x, axis=-1, eps=1e-05):
    m = jnp.mean(x, axis=axis, keepdims=True)
    v = jnp.var(x, axis=axis, keepdims=True)
    return (x - m) / jnp.sqrt(v + eps)

def _scatter_add(tgt, idx, src, axis=0):
    return tgt.at[idx].add(src)

def _segment_sum(src, seg, n):
    return jax.ops.segment_sum(src, seg, n)
kernel_name = 'mk_perceiver_d1_seqx_r2_412ca3'

def setup_inputs(seed: int=0):
    np.random.seed(seed)
    _w = jnp.asarray

    def _rec_inputs():
        import jax
        import jax.numpy as jnp
        _rk = jax.random.key(seed)
        x = -0.0005146 + 1 * jax.random.normal(jax.random.fold_in(_rk, 1), (16, 64, 512), jnp.float32)
        _lenS = 64 - jax.random.randint(jax.random.fold_in(_rk, 7), (16,), 0, max(1, 64 // 4) + 1, jnp.int32)
        _lenS2 = 512 - jax.random.randint(jax.random.fold_in(_rk, 8), (16,), 0, max(1, 512 // 4) + 1, jnp.int32)
        _ctx_1024P = jax.random.normal(jax.random.fold_in(_rk, 11), (16, 16, 512), jnp.float32)
        _ctx_1024c = jax.random.dirichlet(jax.random.fold_in(_rk, 511), 0.3 * jnp.ones((16,), jnp.float32), (16, 512))
        _ctx_1024t = jnp.einsum('bsk,bkd->bsd', _ctx_1024c, _ctx_1024P)
        _ctx_1024t = _ctx_1024t * jax.lax.rsqrt(jnp.mean(jnp.square(_ctx_1024t)) + 1e-12) * 0.953939
        ctx_1024 = -0.000125008 + 0.999885 * (_ctx_1024t + 0.3 * jax.random.normal(jax.random.fold_in(_rk, 611), (16, 512, 512), jnp.float32))
        _validS = jnp.arange(64)[None, :] < _lenS[:, None]
        _validS2 = jnp.arange(512)[None, :] < _lenS2[:, None]
        _causal = jnp.tril(jnp.ones((64, 64), dtype=bool))
        mask_BxS2_bf1 = jnp.ones((16, 512), dtype=bool)
        return (x, ctx_1024, mask_BxS2_bf1)
    x, ctx_1024, mask_BxS2_bf1 = _rec_inputs()

    def _L0_xattn_setup():
        import jax, jax.numpy as jnp
        import numpy as np
        H, DH = (8, 64)
        EPS = 1e-05

        def _ln(x, g, b):
            m = x.mean(-1, keepdims=True)
            v = ((x - m) ** 2).mean(-1, keepdims=True)
            return (x - m) / jnp.sqrt(v + EPS) * g + b
        key = jax.random.key(seed)
        ks = jax.random.split(key, 5)
        B, N, L, D = (4, 4096, 256, 512)
        inner = H * DH
        return {'x': jax.random.normal(ks[0], (B, N, D), jnp.float32), 'latents': jax.random.normal(ks[1], (B, L, D), jnp.float32), 'mask': jnp.ones((B, N), dtype=bool), 'g_x': jnp.ones((D,), jnp.float32), 'b_x': jnp.zeros((D,), jnp.float32), 'g_l': jnp.ones((D,), jnp.float32), 'b_l': jnp.zeros((D,), jnp.float32), 'w_q': jax.random.normal(ks[2], (D, inner), jnp.float32) * D ** (-0.5), 'w_kv': jax.random.normal(ks[3], (D, 2 * inner), jnp.float32) * D ** (-0.5), 'w_out': jax.random.normal(ks[4], (inner, D), jnp.float32) * inner ** (-0.5), 'g_o': jnp.ones((D,), jnp.float32), 'b_o': jnp.zeros((D,), jnp.float32)}
    _L0_xattn_all = _L0_xattn_setup()
    _L0_xattn_in = {k: v for k, v in _L0_xattn_all.items() if k in ('g_x', 'b_x', 'g_l', 'b_l', 'w_q', 'w_kv', 'w_out', 'g_o', 'b_o')}
    del _L0_xattn_all

    def _L0_attn_setup():
        import math
        import jax, jax.numpy as jnp
        import numpy as np
        EMBED_DIM = 512
        NUM_HEADS = 8
        HEAD_DIM = EMBED_DIM // NUM_HEADS // 2
        DEPTH = 12
        LAMBDA_INIT = 0.8 - 0.6 * math.exp(-0.3 * DEPTH)
        B, S = (2, 1024)
        ROPE_THETA = 10000.0
        EPS = 1e-08

        def rope_rotate(x):
            d = x.shape[-1]
            inv_freq = 1.0 / ROPE_THETA ** (jnp.arange(0, d, 2, dtype=jnp.float32) / d)
            t = jnp.arange(x.shape[1], dtype=jnp.float32)
            freqs = t[:, None] * inv_freq[None, :]
            freqs = jnp.repeat(freqs, 2, axis=-1)
            cos = jnp.cos(freqs)[None, :, None, :].astype(x.dtype)
            sin = jnp.sin(freqs)[None, :, None, :].astype(x.dtype)
            xr = x.reshape(*x.shape[:-1], d // 2, 2)
            x1, x2 = (xr[..., 0], xr[..., 1])
            rot = jnp.stack([-x2, x1], axis=-1).reshape(x.shape)
            return x * cos + rot * sin

        def sdpa(q, k, v):
            d = q.shape[-1]
            scores = jnp.einsum('bshd,bthd->bhst', q, k) * d ** (-0.25)
            w = jax.nn.softmax(scores, axis=-1)
            return jnp.einsum('bhst,bthd->bshd', w, v)
        key = jax.random.key(seed)
        ks = jax.random.split(key, 10)
        scale = 1.0 / math.sqrt(EMBED_DIM)
        return {'x': jax.random.normal(ks[0], (B, S, EMBED_DIM), jnp.float32), 'Wq': jax.random.normal(ks[1], (EMBED_DIM, EMBED_DIM), jnp.float32) * scale, 'Wk': jax.random.normal(ks[2], (EMBED_DIM, EMBED_DIM), jnp.float32) * scale, 'Wv': jax.random.normal(ks[3], (EMBED_DIM, EMBED_DIM), jnp.float32) * scale, 'Wo': jax.random.normal(ks[4], (EMBED_DIM, EMBED_DIM), jnp.float32) * scale, 'lambda_q1': jax.random.normal(ks[5], (HEAD_DIM,), jnp.float32) * 0.1, 'lambda_k1': jax.random.normal(ks[6], (HEAD_DIM,), jnp.float32) * 0.1, 'lambda_q2': jax.random.normal(ks[7], (HEAD_DIM,), jnp.float32) * 0.1, 'lambda_k2': jax.random.normal(ks[8], (HEAD_DIM,), jnp.float32) * 0.1, 'ln_w': jnp.ones((2 * HEAD_DIM,), jnp.float32), 'ln_b': jnp.zeros((2 * HEAD_DIM,), jnp.float32)}
    _L0_attn_all = _L0_attn_setup()
    _L0_attn_in = {k: v for k, v in _L0_attn_all.items() if k in ('Wq', 'Wk', 'Wv', 'Wo', 'lambda_q1', 'lambda_k1', 'lambda_q2', 'lambda_k2', 'ln_w', 'ln_b')}
    del _L0_attn_all

    def _L0_ffn_setup():
        import jax, jax.numpy as jnp
        import numpy as np
        BLOCK = 16
        _GRID = jnp.array([0.0, 0.5, 1.0, 1.5, 2.0, 3.0, 4.0, 6.0], dtype=jnp.float32)
        _MID = jnp.array([0.25, 0.75, 1.25, 1.75, 2.5, 3.5, 5.0], dtype=jnp.float32)

        def fp4_quant_dequant(x):
            shape = x.shape
            xb = x.reshape(shape[:-1] + (shape[-1] // BLOCK, BLOCK))
            scale = jnp.max(jnp.abs(xb), axis=-1, keepdims=True) / 6.0
            scale = jnp.maximum(scale, jnp.float32(1e-12))
            xn = xb / scale
            idx = jnp.searchsorted(_MID, jnp.abs(xn))
            q = _GRID[idx] * jnp.sign(xn) * scale
            return q.reshape(shape)

        def fp4_linear(x, w):
            xq = fp4_quant_dequant(x)
            wq = fp4_quant_dequant(w)
            return jnp.einsum('bsk,nk->bsn', xq, wq)
        key = jax.random.key(seed)
        k1, k2, k3, k4 = jax.random.split(key, 4)
        H, I = (512, 1408)
        x = jax.random.normal(k1, (4, 2048, H), dtype=jnp.float32)
        w_gate = jax.random.normal(k2, (I, H), dtype=jnp.float32) * 0.02
        w_up = jax.random.normal(k3, (I, H), dtype=jnp.float32) * 0.02
        w_down = jax.random.normal(k4, (H, I), dtype=jnp.float32) * 0.02
        return {'x': x, 'w_gate': w_gate, 'w_up': w_up, 'w_down': w_down}
    _L0_ffn_all = _L0_ffn_setup()
    _L0_ffn_in = {k: v for k, v in _L0_ffn_all.items() if k in ('w_gate', 'w_up', 'w_down')}
    del _L0_ffn_all
    return {'x': x, 'ctx_1024': ctx_1024, 'mask_BxS2_bf1': mask_BxS2_bf1, 'L0_xattn_g_x': _L0_xattn_in['g_x'], 'L0_xattn_b_x': _L0_xattn_in['b_x'], 'L0_xattn_g_l': _L0_xattn_in['g_l'], 'L0_xattn_b_l': _L0_xattn_in['b_l'], 'L0_xattn_w_q': _L0_xattn_in['w_q'], 'L0_xattn_w_kv': _L0_xattn_in['w_kv'], 'L0_xattn_w_out': _L0_xattn_in['w_out'], 'L0_xattn_g_o': _L0_xattn_in['g_o'], 'L0_xattn_b_o': _L0_xattn_in['b_o'], 'L0_attn_Wq': _L0_attn_in['Wq'], 'L0_attn_Wk': _L0_attn_in['Wk'], 'L0_attn_Wv': _L0_attn_in['Wv'], 'L0_attn_Wo': _L0_attn_in['Wo'], 'L0_attn_lambda_q1': _L0_attn_in['lambda_q1'], 'L0_attn_lambda_k1': _L0_attn_in['lambda_k1'], 'L0_attn_lambda_q2': _L0_attn_in['lambda_q2'], 'L0_attn_lambda_k2': _L0_attn_in['lambda_k2'], 'L0_attn_ln_w': _L0_attn_in['ln_w'], 'L0_attn_ln_b': _L0_attn_in['ln_b'], 'L0_ffn_w_gate': _L0_ffn_in['w_gate'], 'L0_ffn_w_up': _L0_ffn_in['w_up'], 'L0_ffn_w_down': _L0_ffn_in['w_down']}

def reference(x, ctx_1024, mask_BxS2_bf1, L0_xattn_g_x, L0_xattn_b_x, L0_xattn_g_l, L0_xattn_b_l, L0_xattn_w_q, L0_xattn_w_kv, L0_xattn_w_out, L0_xattn_g_o, L0_xattn_b_o, L0_attn_Wq, L0_attn_Wk, L0_attn_Wv, L0_attn_Wo, L0_attn_lambda_q1, L0_attn_lambda_k1, L0_attn_lambda_q2, L0_attn_lambda_k2, L0_attn_ln_w, L0_attn_ln_b, L0_ffn_w_gate, L0_ffn_w_up, L0_ffn_w_down):
    import jax
    import jax.numpy as jnp

    def _L0_xattn_ref(x, latents, mask, g_x, b_x, g_l, b_l, w_q, w_kv, w_out, g_o, b_o):
        import jax, jax.numpy as jnp
        import numpy as np
        H, DH = (8, 64)
        EPS = 1e-05

        def _ln(x, g, b):
            m = x.mean(-1, keepdims=True)
            v = ((x - m) ** 2).mean(-1, keepdims=True)
            return (x - m) / jnp.sqrt(v + EPS) * g + b
        B, Lq = (latents.shape[0], latents.shape[1])
        scale = DH ** (-0.5)
        xn = _ln(x, g_x, b_x)
        ln = _ln(latents, g_l, b_l)
        q = ln @ w_q
        kv_in = jnp.concatenate([xn, ln], axis=1)
        k, v = jnp.split(kv_in @ w_kv, 2, axis=-1)
        split = lambda t: t.reshape(t.shape[0], t.shape[1], H, DH).transpose(0, 2, 1, 3)
        q, k, v = (split(q) * scale, split(k), split(v))
        sim = jnp.einsum('bhid,bhjd->bhij', q, k)
        m = jnp.concatenate([mask, jnp.ones((B, Lq), dtype=bool)], axis=1)[:, None, None, :]
        sim = jnp.where(m, sim, -jnp.finfo(sim.dtype).max)
        attn = jax.nn.softmax(sim, axis=-1)
        out = jnp.einsum('bhij,bhjd->bhid', attn, v)
        out = out.transpose(0, 2, 1, 3).reshape(B, Lq, H * DH)
        return _ln(out @ w_out, g_o, b_o)

    def _L0_attn_ref(x, Wq, Wk, Wv, Wo, lambda_q1, lambda_k1, lambda_q2, lambda_k2, ln_w, ln_b):
        import math
        import jax, jax.numpy as jnp
        import numpy as np
        EMBED_DIM = 512
        NUM_HEADS = 8
        HEAD_DIM = EMBED_DIM // NUM_HEADS // 2
        DEPTH = 12
        LAMBDA_INIT = 0.8 - 0.6 * math.exp(-0.3 * DEPTH)
        B, S = (2, 1024)
        ROPE_THETA = 10000.0
        EPS = 1e-08

        def rope_rotate(x):
            d = x.shape[-1]
            inv_freq = 1.0 / ROPE_THETA ** (jnp.arange(0, d, 2, dtype=jnp.float32) / d)
            t = jnp.arange(x.shape[1], dtype=jnp.float32)
            freqs = t[:, None] * inv_freq[None, :]
            freqs = jnp.repeat(freqs, 2, axis=-1)
            cos = jnp.cos(freqs)[None, :, None, :].astype(x.dtype)
            sin = jnp.sin(freqs)[None, :, None, :].astype(x.dtype)
            xr = x.reshape(*x.shape[:-1], d // 2, 2)
            x1, x2 = (xr[..., 0], xr[..., 1])
            rot = jnp.stack([-x2, x1], axis=-1).reshape(x.shape)
            return x * cos + rot * sin

        def sdpa(q, k, v):
            d = q.shape[-1]
            scores = jnp.einsum('bshd,bthd->bhst', q, k) * d ** (-0.25)
            w = jax.nn.softmax(scores, axis=-1)
            return jnp.einsum('bhst,bthd->bshd', w, v)
        b, s, e = x.shape
        H, D = (NUM_HEADS, HEAD_DIM)
        q = (x @ Wq.T).reshape(b, s, 2 * H, D)
        k = (x @ Wk.T).reshape(b, s, 2 * H, D)
        v = (x @ Wv.T).reshape(b, s, H, 2, D)
        q = rope_rotate(q).reshape(b, s, H, 2, D)
        k = rope_rotate(k).reshape(b, s, H, 2, D)
        q1, q2 = (q[..., 0, :], q[..., 1, :])
        k1, k2 = (k[..., 0, :], k[..., 1, :])
        v1, v2 = (v[..., 0, :], v[..., 1, :])
        attn1 = sdpa(q1, k1, v1)
        attn2 = sdpa(q2, k2, v2)
        lam = jnp.exp(jnp.sum(lambda_q1 * lambda_k1)) - jnp.exp(jnp.sum(lambda_q2 * lambda_k2)) + LAMBDA_INIT
        diff = jnp.concatenate([attn1, attn2], axis=0)
        a = attn1 - lam * attn2
        a2 = jnp.concatenate([attn1[..., None, :], attn2[..., None, :]], axis=-2)
        a2 = a2[..., 0, :] - lam * a2[..., 1, :]
        attn1f = sdpa(q1, k1, jnp.concatenate([v1, v2], axis=-1) * 0 + jnp.concatenate([v1, v2], axis=-1))
        vfull = jnp.concatenate([v1, v2], axis=-1)
        o1 = sdpa(q1, k1, vfull)
        o2 = sdpa(q2, k2, vfull)
        o = o1 - lam * o2
        ms = jnp.mean(jnp.square(o), axis=-1, keepdims=True)
        o = o * jax.lax.rsqrt(ms + EPS) * ln_w + ln_b
        o = o * (1.0 - LAMBDA_INIT)
        o = o.reshape(b, s, e)
        return o @ Wo.T

    def _L0_ffn_ref(x, w_gate, w_up, w_down):
        import jax, jax.numpy as jnp
        import numpy as np
        BLOCK = 16
        _GRID = jnp.array([0.0, 0.5, 1.0, 1.5, 2.0, 3.0, 4.0, 6.0], dtype=jnp.float32)
        _MID = jnp.array([0.25, 0.75, 1.25, 1.75, 2.5, 3.5, 5.0], dtype=jnp.float32)

        def fp4_quant_dequant(x):
            shape = x.shape
            xb = x.reshape(shape[:-1] + (shape[-1] // BLOCK, BLOCK))
            scale = jnp.max(jnp.abs(xb), axis=-1, keepdims=True) / 6.0
            scale = jnp.maximum(scale, jnp.float32(1e-12))
            xn = xb / scale
            idx = jnp.searchsorted(_MID, jnp.abs(xn))
            q = _GRID[idx] * jnp.sign(xn) * scale
            return q.reshape(shape)

        def fp4_linear(x, w):
            xq = fp4_quant_dequant(x)
            wq = fp4_quant_dequant(w)
            return jnp.einsum('bsk,nk->bsn', xq, wq)
        gate = fp4_linear(x, w_gate)
        y = fp4_linear(x, w_up)
        h = jax.nn.silu(gate) * y
        return fp4_linear(h, w_down)
    x = x + _L0_xattn_ref(ctx_1024, _layernorm(x, axis=-1), mask_BxS2_bf1, L0_xattn_g_x, L0_xattn_b_x, L0_xattn_g_l, L0_xattn_b_l, L0_xattn_w_q, L0_xattn_w_kv, L0_xattn_w_out, L0_xattn_g_o, L0_xattn_b_o)
    x = x + _L0_attn_ref(_layernorm(x, axis=-1), L0_attn_Wq, L0_attn_Wk, L0_attn_Wv, L0_attn_Wo, L0_attn_lambda_q1, L0_attn_lambda_k1, L0_attn_lambda_q2, L0_attn_lambda_k2, L0_attn_ln_w, L0_attn_ln_b)
    x = x + _L0_ffn_ref(_layernorm(x, axis=-1), L0_ffn_w_gate, L0_ffn_w_up, L0_ffn_w_down)
    return x

_drawn_inputs = setup_inputs


def setup_inputs(seed=0):
    import zlib

    import numpy as np

    out = dict(_drawn_inputs(seed))
    spreads = {'L0_xattn_g_x': (1.0, 0.2),
     'L0_xattn_b_x': (0.0, 0.1),
     'L0_xattn_g_l': (1.0, 0.2),
     'L0_xattn_b_l': (0.0, 0.1),
     'L0_xattn_g_o': (1.0, 0.2),
     'L0_xattn_b_o': (0.0, 0.1),
     'L0_attn_ln_w': (1.0, 0.2),
     'L0_attn_ln_b': (0.0, 0.441)}
    factors = {'L0_attn_lambda_q1': 2.879,
     'L0_attn_lambda_k1': 6.16,
     'L0_attn_lambda_q2': 64.0,
     'L0_attn_lambda_k2': 64.0}
    for name, (base, spread) in spreads.items():
        noise = np.random.default_rng([zlib.crc32(name.encode()), seed]).standard_normal(out[name].shape)
        drawn = base * np.exp(spread * noise) if base else spread * noise
        out[name] = jnp.asarray(drawn.astype(out[name].dtype))
    for name, factor in factors.items():
        out[name] = (out[name] * factor).astype(out[name].dtype)
    return out
```

```python
import math
from contextlib import ExitStack

import numpy as np
import concourse.bass as bass
from concourse import mybir

F32 = mybir.dt.float32
F32R = mybir.dt.float32r
BF16 = mybir.dt.bfloat16
U8 = mybir.dt.uint8
U16 = mybir.dt.uint16
U32 = mybir.dt.uint32
ALU = mybir.AluOpType
ACT = mybir.ActivationFunctionType
AX = mybir.AxisListType

P = 128
NB, LQ, S, D = 16, 64, 512, 512
H, DH = 8, 64
T = NB * LQ
NT = T // P
C = D // P
CS = S // P
INNER = 1408
CI = INNER // P
EPS_LN = 1e-5
EPS_RMS = 1e-8
HALF = 512
LAMBDA_INIT = 0.8 - 0.6 * math.exp(-0.3 * 12)
DD = 32
SCORE_SCALE = float(DD) ** -0.25
F32_MAX = 3.4028234663852886e38
QB = 16
SIXTH = float(np.float32(1.0) / np.float32(6.0))


class Queue:

    def __init__(self, sem):
        self.sem, self.count, self.items = sem, 0, []

    def put(self, after, issue):
        self.count += 1
        self.items.append((list(tokens(after)), issue, self.sem, 1))
        return (self.sem, self.count)

    def dma(self, after, transfers, landed):
        for i, t in enumerate(transfers):
            self.items.append((list(tokens(after)) if i == 0 else [], t, landed[0], 16))
        landed[1] += 16 * len(transfers)
        return (landed[0], landed[1])

    def emit(self, engine):
        seen = {}
        for after, issue, sem, inc in self.items:
            for s, v in after:
                if seen.get(id(s), 0) < v:
                    engine.wait_ge(s, v)
                    seen[id(s)] = v
            issue(engine).then_inc(sem, inc)


def copy_bits(e, dst, src):
    as_words = [x.bitcast(F32) if x.dtype == F32R else x for x in (dst, src)]
    return e.dma_start(*as_words)


def tokens(after):
    if after is None:
        return
    if isinstance(after, tuple) and isinstance(after[1], int):
        yield after
        return
    for a in after:
        yield from tokens(a)


def over(ap, n):
    return ap.unsqueeze(2).to_broadcast([ap.shape[0], ap.shape[1], n])


def blocks(ap, n):
    return ap.rearrange("p (b e) -> p b e", e=n)


def perceiver(nc, a, out):
    ctx = ExitStack()
    with ctx:
        def sem(name):
            return ctx.enter_context(nc.semaphore(name))

        pe, dve, act, pool = (Queue(sem(n)) for n in ("pe_done", "dve_done", "act_done", "pool_done"))
        sp = Queue(sem("sp_done"))

        def stream(name):
            return [sem(name), 0]

        def sb(scope, name, shape, dt=F32):
            return scope.enter_context(nc.sbuf_tensor("sb_" + name, shape, dt))

        psum = ctx.enter_context(nc.psum_tensor("ps_banks", [P, 8, 512], F32))

        def flat(first, last):
            return psum[:, first:last, :].rearrange("p b n -> p (b n)")

        def scratch(name, shape, dt):
            return nc.dram_tensor("scratch_" + name, shape, dt, kind="Internal").ap()

        q_spill = scratch("q", [NB, P, C, 2, P], F32)
        klat_spill = scratch("klat", [NB, P, C, 2, LQ], F32)
        vlat_spill = scratch("vlat", [T, D], F32)
        wgu_spill = scratch("wgu", [2, 2, P, C, INNER], F32)
        wdn_spill = scratch("wdn", [2, P, CI, D], F32)

        ident = sb(ctx, "ident", [P, P])
        stacked = sb(ctx, "stacked", [P, LQ])
        half_pow = sb(ctx, "half_pow", [P, NT])
        cols = sb(ctx, "cols", [P, 4, C])
        c_load = stream("c_landed")
        consts = sp.dma([], [
            lambda e: copy_bits(e, ident[:, :], a["ident"]),
            lambda e: copy_bits(e, stacked[:, :], a["stacked"]),
            lambda e: copy_bits(e, cols[:, :, :], a["cols"]),
        ], c_load)
        pow_set = dve.put([], lambda e: e.memset(half_pow[:, :], -0.5))

        def mm3(e, o, w, x, chunks, start=True, stop=True):
            n = len(chunks)
            for i, c in enumerate(chunks):
                (wh, wl), (xh, xl) = w(c), x(c)
                e.matmul(o, wh, xh, start=start and i == 0, stop=False)
                e.matmul(o, wh, xl, start=False, stop=False)
                m = e.matmul(o, wl, xh, start=False, stop=stop and i == n - 1)
            return m

        def layernorm(src, dst, n, st, after, free_small=None, eps=EPS_LN, scale_q=None):
            stats, mv, ve, rstd = st
            for i in range(n):
                s = dve.put([after, free_small] if i == 0 else (after[i] if isinstance(after, list) and len(after) == n else []),
                            lambda e, i=i: e.bn_stats(stats[:, i, :], src(i)))
            for i in range(n):
                s = dve.put([s] if i == 0 else [], lambda e, i=i: e.bn_aggr(mv[:, i, :], stats[:, i, :]))
            s = dve.put([s], lambda e: e.tensor_scalar(ve[:, 0:n], mv[:, 0:n, 1], eps, None, ALU.add))
            s = pool.put([s, pow_set], lambda e: e.tensor_tensor(rstd[:, 0:n], ve[:, 0:n], half_pow[:, 0:n], ALU.pow))
            done = []
            for i in range(n):
                done.append((scale_q or dve).put([s], lambda e, i=i: e.tensor_scalar(
                    dst(i), src(i), mv[:, i, 0:1], rstd[:, i:i + 1], ALU.subtract, ALU.mult)))
            return done

        def ln_small(scope, name, n):
            return (sb(scope, name + "_stats", [P, n, 6]), sb(scope, name + "_mv", [P, n, 2]),
                    sb(scope, name + "_ve", [P, n]), sb(scope, name + "_rstd", [P, n]))

        def split(full, hi, lo, after):
            h = act.put(after, lambda e: e.activation(hi, full, ACT.Identity))
            return h, dve.put([after, h], lambda e: e.tensor_tensor(lo, full, hi.bitcast(F32), ALU.subtract))

        class Quantiser:

            def __init__(self, scope, name, width):
                nb = width // QB
                self.amax = sb(scope, name + "_amax", [P, nb])
                self.scale = sb(scope, name + "_scale", [P, nb])
                self.inv = sb(scope, name + "_inv", [P, nb])
                self.xn = sb(scope, name + "_xn", [P, width])
                self.mag = sb(scope, name + "_mag", [P, width], U16)
                self.lo = sb(scope, name + "_lo", [P, width], BF16)
                self.mid = sb(scope, name + "_mid", [P, width], BF16)
                self.top = sb(scope, name + "_top", [P, width], BF16)

            def run(self, x, q, n, after, free_q=None):
                nb = n // QB
                amax, scale, inv = self.amax[:, 0:nb], self.scale[:, 0:nb], self.inv[:, 0:nb]
                xn, mag = self.xn[:, 0:n], self.mag[:, 0:n]
                lo, mid, top = self.lo[:, 0:n], self.mid[:, 0:n], self.top[:, 0:n]
                magf = mag.bitcast(BF16)
                upper = xn.bitcast(U16).rearrange("p (n t) -> p n t", t=2)[:, :, 1]
                s = dve.put([after], lambda e: e.tensor_reduce(
                    amax, blocks(x, QB), AX.X, ALU.max, apply_absolute_value=True))
                s = dve.put([s], lambda e: e.tensor_scalar(scale, amax, SIXTH, 1e-12, ALU.mult, ALU.max))
                s = dve.put([s], lambda e: e.reciprocal(inv, scale))
                s = dve.put([s], lambda e: e.scalar_tensor_tensor(
                    out=blocks(xn, QB), in0=blocks(x, QB), scalar=float(1 - 2.0 ** -24),
                    in1=over(inv, QB), op0=ALU.mult, op1=ALU.mult))
                s = dve.put([s], lambda e: e.tensor_scalar(mag, upper, 0x7FFE, 1, ALU.bitwise_and, ALU.bitwise_or))
                dve.put([s], lambda e: e.tensor_scalar(lo, magf, 2.0, 64.0, ALU.min, ALU.add))
                m = dve.put([], lambda e: e.tensor_scalar(mid, magf, 2.0, 4.0, ALU.max, ALU.min))
                dve.put([], lambda e: e.tensor_scalar(top, magf, 4.0, 252.0, ALU.max, ALU.add))
                s = dve.put([m], lambda e: e.tensor_scalar(mid, mid, 126.0, None, ALU.add))
                s = dve.put([s], lambda e: e.scalar_tensor_tensor(
                    out=mid, in0=lo, scalar=-192.0, in1=mid, op0=ALU.add, op1=ALU.add))
                s = dve.put([s], lambda e: e.scalar_tensor_tensor(
                    out=top, in0=top, scalar=-256.0, in1=mid, op0=ALU.add, op1=ALU.add))
                s = dve.put([s, free_q], lambda e: e.tensor_tensor(
                    blocks(q, QB), blocks(top, QB), over(scale, QB), ALU.mult))
                return dve.put([s], lambda e: e.scalar_tensor_tensor(
                    out=q.bitcast(U32), in0=xn.bitcast(U32), scalar=0x80000000, in1=q.bitcast(U32),
                    op0=ALU.bitwise_and, op1=ALU.bitwise_or))

        attn_t = sb(ctx, "attnT", [P, C, T])
        stage_b = ExitStack()
        wkv_hi = sb(stage_b, "wkv_hi", [P, C, 2 * D], F32R)
        wkv_lo = sb(stage_b, "wkv_lo", [P, C, 2 * D], F32R)
        stage_a = ExitStack()
        x_in = sb(stage_a, "a_x", [P, NT, D])
        w_raw = sb(stage_a, "a_wraw", [P, C, 2 * D])
        wq_hi = sb(stage_a, "a_wq_hi", [P, C, D], F32R)
        wq_lo = sb(stage_a, "a_wq_lo", [P, C, D], F32R)
        ln_t = sb(stage_a, "a_lnT", [P, HALF])
        ln_hi = sb(stage_a, "a_lnT_hi", [P, C, HALF], F32R)
        ln_lo = sb(stage_a, "a_lnT_lo", [P, C, HALF], F32R)
        q_stage = [[sb(stage_a, f"a_q{i}{part}", [P, HALF // LQ, P], F32R) for part in ("hi", "lo")] for i in range(2)]
        k_stage = [[sb(stage_a, f"a_k{i}{part}", [P, HALF], F32R) for part in ("hi", "lo")] for i in range(2)]
        v_stage = [sb(stage_a, f"a_v{i}", [P, D]) for i in range(2)]
        small_a = ln_small(stage_a, "a", NT)
        a_load = [stream("a_x_landed"), stream("a_wq_landed"), stream("a_wkv_landed")]
        x_landed = sp.dma([], [lambda e: copy_bits(e, x_in[:, :, :], a["x"].rearrange("(t p) d -> p t d", p=P))], a_load[0])
        wq_landed = sp.dma([], [lambda e: copy_bits(e, w_raw[:, :, 0:D], a["w_q"].rearrange("(c p) n -> p c n", p=P))], a_load[1])
        w_split = split(w_raw[:, :, 0:D], wq_hi[:, :, :], wq_lo[:, :, :], [wq_landed])
        wkv_landed = sp.dma([w_split], [lambda e: copy_bits(e, w_raw[:, :, :], a["w_kv"].rearrange("(c p) n -> p c n", p=P))], a_load[2])
        zeroed = [dve.put([], lambda e, q=q: e.memset(q[:, :, :].bitcast(U32), 0)) for qs in q_stage for q in qs]

        z1 = layernorm(lambda i: x_in[:, i, :], lambda i: x_in[:, i, :], NT, small_a, [x_landed])
        z2 = layernorm(lambda i: x_in[:, i, :], lambda i: x_in[:, i, :], NT, small_a, [z1])
        wkv_split = split(w_raw[:, :, :], wkv_hi[:, :, :], wkv_lo[:, :, :], [wkv_landed])

        bank_free = [None] * 8
        q_out = [stream(f"q_spilled{i}") for i in range(2)]
        k_out = [stream(f"klat_spilled{i}") for i in range(2)]
        v_out = [stream(f"vlat_spilled{i}") for i in range(2)]
        stage_free = {}
        spilled = []
        turn = 0
        ln_reads = []
        for half in range(2):
            ln_ready = []
            affine = None
            for c in range(C):
                bank = c % 2
                tr = pe.put([z2, consts, bank_free[bank]], lambda e, c=c, half=half, bank=bank: [
                    e.transpose(psum[:, bank, k * P:(k + 1) * P], x_in[:, 4 * half + k, c * P:(c + 1) * P], ident[:, :])
                    for k in range(4)][-1])
                affine = act.put([tr, ln_ready, consts], lambda e, c=c, bank=bank: e.activation(
                    ln_t[:, :], psum[:, bank, :], ACT.Identity, bias=cols[:, 3, c:c + 1], scale=cols[:, 2, c:c + 1]))
                bank_free[bank] = affine
                hi = act.put([affine, ln_reads], lambda e, c=c: e.activation(ln_hi[:, c, :], ln_t[:, :], ACT.Identity))
                ln_ready.append(dve.put([hi], lambda e, c=c: e.tensor_tensor(
                    ln_lo[:, c, :], ln_t[:, :], ln_hi[:, c, :].bitcast(F32), ALU.subtract)))
            ln_reads = []

            def latents(c):
                return ln_hi[:, c, :], ln_lo[:, c, :]

            for n in range(C):
                bank, slot = 2 + turn % 4, turn % 2
                turn += 1
                cs = slice(n * P, (n + 1) * P)
                mm = pe.put([ln_ready, w_split, bank_free[bank]], lambda e, bank=bank, cs=cs: mm3(
                    e, psum[:, bank, :], lambda c: (wq_hi[:, c, cs], wq_lo[:, c, cs]), latents, range(C)))
                ln_reads.append(mm)
                qh, ql = q_stage[slot]
                parts = [(slice(0, 64), slice(0, 64)), (slice(64, 128), slice(64, 128))]
                his = [act.put([mm, zeroed, stage_free.get(("q", slot))], lambda e, r=r, k=k, bank=bank, qh=qh: e.activation(
                    qh[r, :, k], blocks(psum[r, bank, :], LQ), ACT.Copy, scale=DH ** -0.5)) for r, k in parts]
                los = [dve.put([mm, his], lambda e, r=r, k=k, bank=bank, qh=qh, ql=ql: e.scalar_tensor_tensor(
                    out=ql[r, :, k], in0=blocks(psum[r, bank, :], LQ), scalar=DH ** -0.5,
                    in1=qh[r, :, k].bitcast(F32), op0=ALU.mult, op1=ALU.subtract)) for r, k in parts]
                bank_free[bank] = los[-1]
                b0 = half * (NB // 2)
                stage_free[("q", slot)] = sp.dma([los], [lambda e, n=n, b0=b0, i=i, s=s: copy_bits(e, 
                    q_spill[b0:b0 + NB // 2, :, n, i, :].rearrange("b p k -> p b k"), s[:, :, :])
                    for i, s in enumerate((qh, ql))], q_out[slot])
                spilled.append(stage_free[("q", slot)])
            for n in range(C):
                bank, slot = 2 + turn % 4, turn % 2
                turn += 1
                cs = slice(n * P, (n + 1) * P)
                mm = pe.put([ln_ready, wkv_split, bank_free[bank]], lambda e, bank=bank, cs=cs: mm3(
                    e, psum[:, bank, :], lambda c: (wkv_hi[:, c, cs], wkv_lo[:, c, cs]), latents, range(C)))
                ln_reads.append(mm)
                kh, kl = k_stage[slot]
                s = split(psum[:, bank, :], kh[:, :], kl[:, :], [mm, stage_free.get(("k", slot))])
                bank_free[bank] = s[1]
                b0 = half * (NB // 2)
                stage_free[("k", slot)] = sp.dma([s], [lambda e, n=n, b0=b0, i=i, s=s_: copy_bits(e, 
                    klat_spill[b0:b0 + NB // 2, :, n, i, :].rearrange("b p k -> p b k"), blocks(s[:, :], LQ))
                    for i, s_ in enumerate((kh, kl))], k_out[slot])
                spilled.append(stage_free[("k", slot)])
            for k in range(4):
                bank, slot = 2 + turn % 4, turn % 2
                turn += 1
                ts = slice(k * P, (k + 1) * P)
                mm = pe.put([ln_ready, wkv_split, bank_free[bank]], lambda e, bank=bank, ts=ts: mm3(
                    e, psum[:, bank, :], lambda c: (ln_hi[:, c, ts], ln_lo[:, c, ts]),
                    lambda c: (wkv_hi[:, c, D:2 * D], wkv_lo[:, c, D:2 * D]), range(C)))
                ln_reads.append(mm)
                cp = act.put([mm, stage_free.get(("v", slot))], lambda e, bank=bank, slot=slot: e.activation(
                    v_stage[slot][:, :], psum[:, bank, :], ACT.Identity))
                bank_free[bank] = cp
                t = 4 * half + k
                stage_free[("v", slot)] = sp.dma([cp], [lambda e, t=t, slot=slot: copy_bits(e, 
                    vlat_spill[t * P:(t + 1) * P, :], v_stage[slot][:, :])], v_out[slot])
                spilled.append(stage_free[("v", slot)])
        stage_a.close()
        a_done = [spilled, bank_free, ln_reads, (pe.sem, pe.count), (act.sem, act.count), (dve.sem, dve.count)]

        ctx_in = [sb(stage_b, f"ctx{i}", [P, CS, D]) for i in range(2)]
        z_full = [sb(stage_b, f"zfull{i}", [P, S]) for i in range(2)]
        z_hi = [sb(stage_b, f"zT_hi{i}", [P, C, S], F32R) for i in range(2)]
        z_lo = [sb(stage_b, f"zT_lo{i}", [P, C, S], F32R) for i in range(2)]
        k_hi = sb(stage_b, "kT_hi", [P, C, S], F32R)
        k_lo = sb(stage_b, "kT_lo", [P, C, S], F32R)
        v_sb = [sb(stage_b, f"v{i}", [P, CS, D]) for i in range(2)]
        q_pack = [sb(stage_b, f"qpack{i}", [P, C, 2, P], F32R) for i in range(2)]
        kl_pack = [sb(stage_b, f"klpack{i}", [P, C, 2, LQ], F32R) for i in range(2)]
        vl_pack = [sb(stage_b, f"vlpack{i}", [LQ, D]) for i in range(2)]
        probs = [sb(stage_b, f"probs{i}", [P, S + LQ]) for i in range(2)]
        p_t = [sb(stage_b, f"probsT{i}", [P, CS + 1, P]) for i in range(2)]
        o_diag = sb(stage_b, "o_diag", [P, C, P])
        mask_in = [sb(stage_b, f"mask{i}", [P, S], U8) for i in range(2)]
        mask_bias = [sb(stage_b, f"maskbias{i}", [P, S + LQ]) for i in range(2)]
        neg_max = sb(stage_b, "neg_max", [P, C])
        row_sum = [sb(stage_b, f"row_sum{i}", [P, C]) for i in range(2)]
        row_inv = sb(stage_b, "row_inv", [P, C])
        small_b = ln_small(stage_b, "b", CS)
        b_load = {k: [stream(f"{k}_landed{i}") for i in range(2)] for k in ("ctx", "pack")}
        s_space = [flat(0, 2), flat(2, 4)]
        lat_pt = [psum[0:LQ, 2 * j + 1, 256:256 + P] for j in range(2)]

        init = dve.put([a_done], lambda e: e.memset(o_diag[:, :, :], 0.0))
        for i in range(2):
            init = dve.put([], lambda e, i=i: e.memset(mask_bias[i][:, :], 0.0))

        st = {}
        free = {}

        turns = [0]

        def next_bank():
            turns[0] += 1
            bank = 4 + turns[0] % 4
            return bank, free.get(("bank", bank))

        def load_batch(b):
            i = b % 2
            st["ctx", b] = sp.dma([a_done, free.get(("ctx", i))], [
                lambda e: copy_bits(e, ctx_in[i][:, :, :], a["ctx"][b].rearrange("(p s) d -> p s d", p=P)),
                lambda e: copy_bits(e, mask_in[i][:, :], a["mask"][b].partition_broadcast(P)),
            ], b_load["ctx"][i])

        def load_pack(b):
            i = b % 2
            st["pack", b] = sp.dma([a_done, free.get(("pack", i))], [
                lambda e: copy_bits(e, q_pack[i][:, :, :, :], q_spill[b]),
                lambda e: copy_bits(e, kl_pack[i][:, :, :, :], klat_spill[b]),
                lambda e: copy_bits(e, vl_pack[i][:, :], vlat_spill[b * LQ:(b + 1) * LQ, :]),
            ], b_load["pack"][i])

        def normalise(b):
            i = b % 2
            st["z", b] = layernorm(lambda k: ctx_in[i][:, k, :], lambda k: ctx_in[i][:, k, :], CS, small_b,
                                   [st["ctx", b]], free_small=[st.get(("z", b - 1)), init])
            st["mask", b] = dve.put([st["ctx", b], free.get(("maskbias", i)), init], lambda e: e.tensor_scalar(
                mask_bias[i][:, 0:S], mask_in[i][:, :], -1.0, F32_MAX, ALU.add, ALU.mult))

        def transpose_z(b, c):
            i, j = b % 2, c % 2
            bank, bank_read = next_bank()
            tr = pe.put([st["z", b], bank_read, a_done], lambda e: [
                e.transpose(psum[:, bank, k * P:(k + 1) * P], ctx_in[i][:, k, c * P:(c + 1) * P], ident[:, :])
                for k in range(CS)][-1])
            if c == C - 1:
                free["ctx", i] = [tr, st["mask", b]]
            full = act.put([tr, free.get(("zfull", j))], lambda e: e.activation(
                z_full[j][:, :], psum[:, bank, :], ACT.Identity, bias=cols[:, 1, c:c + 1], scale=cols[:, 0, c:c + 1]))
            free["bank", bank] = full
            hi = dve.put([full, free.get(("zT", i))], lambda e: e.tensor_copy(z_hi[i][:, c, :], z_full[j][:, :]))
            lo = dve.put([hi], lambda e: e.tensor_tensor(
                z_lo[i][:, c, :], z_full[j][:, :], z_hi[i][:, c, :].bitcast(F32), ALU.subtract))
            free["zfull", j] = lo
            st["zT", b, c] = lo

        def project_k(b, n):
            i, cs = b % 2, slice(n * P, (n + 1) * P)
            bank, bank_read = next_bank()
            mm = pe.put([[st["zT", b, c] for c in range(C)], bank_read], lambda e: mm3(
                e, psum[:, bank, :], lambda c: (wkv_hi[:, c, cs], wkv_lo[:, c, cs]),
                lambda c: (z_hi[i][:, c, :], z_lo[i][:, c, :]), range(C)))
            hi, lo = split(psum[:, bank, :], k_hi[:, n, :], k_lo[:, n, :], [mm, free.get(("k", n))])
            free["bank", bank] = lo
            st["k", b, n] = [hi, lo]

        def project_v(b, k):
            i, ts = b % 2, slice(k * P, (k + 1) * P)
            bank, bank_read = next_bank()
            mm = pe.put([bank_read], lambda e: mm3(
                e, psum[:, bank, :], lambda c: (z_hi[i][:, c, ts], z_lo[i][:, c, ts]),
                lambda c: (wkv_hi[:, c, D:2 * D], wkv_lo[:, c, D:2 * D]), range(C)))
            if k % 2:
                cp = act.put([mm, free.get(("v", i))], lambda e: e.activation(v_sb[i][:, k, :], psum[:, bank, :], ACT.Identity))
            else:
                cp = dve.put([mm, free.get(("v", i))], lambda e: e.tensor_copy(v_sb[i][:, k, :], psum[:, bank, :]))
            free["bank", bank] = cp
            st["v", b, k] = cp
            if k == CS - 1:
                free["zT", i] = mm

        def scores(b, n):
            i, j = b % 2, n % 2
            q = (q_pack[i][:, n, 0, :], q_pack[i][:, n, 1, :])
            pe.put([st["k", b, n], st["pack", b], free.get(("s", j))], lambda e: mm3(
                e, s_space[j][:, 0:S], lambda c: q, lambda c: (k_hi[:, n, :], k_lo[:, n, :]), range(1)))
            mm = pe.put([free.get(("lat_pt", j))], lambda e: mm3(
                e, s_space[j][:, S:S + LQ], lambda c: q,
                lambda c: (kl_pack[i][:, n, 0, :], kl_pack[i][:, n, 1, :]), range(1)))
            free["k", n] = mm
            mx = dve.put([mm, st["mask", b], free.get(("probs", j))], lambda e: e.tensor_tensor_reduce(
                probs[j][:, :], s_space[j][:, 0:S + LQ], mask_bias[i][:, :], -1.0, F32_MAX, ALU.add, ALU.min, neg_max[:, n:n + 1]))
            free["s", j] = mx
            if n == C - 1:
                free["maskbias", i] = mx
            st["p", b, n] = act.put([mx, free.get(("row_sum", i)) if n == 0 else None], lambda e: e.activation(
                probs[j][:, :], probs[j][:, :], ACT.Exp, bias=neg_max[:, n:n + 1], scale=-1.0,
                accum_out=row_sum[i][:, n:n + 1]))

        def transpose_p(b, n):
            j = n % 2
            bank, bank_read = next_bank()

            def issue(e):
                for k in range(CS):
                    e.transpose(psum[:, bank, k * P:(k + 1) * P], probs[j][:, k * P:(k + 1) * P], ident[:, :])
                return e.transpose(lat_pt[j], probs[j][:, S:S + LQ], ident[:, :])
            tr = pe.put([st["p", b, n], bank_read], issue)
            free["probs", j] = tr
            main = act.put([tr, free.get(("p_t", j))], lambda e: e.activation(
                p_t[j][:, 0:CS, :].rearrange("p c n -> p (c n)"), psum[:, bank, :], ACT.Identity))
            tail = dve.put([tr, free.get(("p_t", j))], lambda e: e.tensor_copy(p_t[j][0:LQ, CS, :], lat_pt[j]))
            free["bank", bank], free["lat_pt", j] = main, tail
            st["pT", b, n] = [main, tail]

        def weigh_v(b, n):
            i, j, cs = b % 2, n % 2, slice(n * P, (n + 1) * P)

            bank, bank_read = next_bank()
            o = psum[:, bank, 0:P]

            def issue(e):
                for k in range(CS):
                    e.matmul(o, p_t[j][:, k, :], v_sb[i][:, k, cs], start=k == 0, stop=False)
                return e.matmul(o, p_t[j][0:LQ, CS, :], vl_pack[i][:, cs], start=False, stop=True)
            mm = pe.put([st["pT", b, n], [st["v", b, k] for k in range(CS)], bank_read], issue)
            free["p_t", j] = mm
            if n == C - 1:
                free["v", i] = mm
                free["pack", i] = mm
            r = dve.put([st["p", b, n], free.get(("row_inv", n))], lambda e: e.reciprocal(
                row_inv[:, n:n + 1], row_sum[i][:, n:n + 1]))
            free["row_sum", i] = r
            ds = [dve.put([r, mm, free.get("o_diag"), init], lambda e, r_=r_: e.tensor_scalar(
                o_diag[r_, n, r_], psum[r_, bank, r_], row_inv[r_, n:n + 1], None, ALU.mult))
                for r_ in (slice(0, 64), slice(64, 128))]
            free["bank", bank] = free["row_inv", n] = ds
            st["o", b, n] = ds

        def turn_o(b):
            bank, bank_read = next_bank()
            ot = psum[:, bank, 0:C * LQ]
            mm = pe.put([[st["o", b, n] for n in range(C)], bank_read], lambda e: [e.matmul(
                ot[:, n * LQ:(n + 1) * LQ], o_diag[:, n, :], stacked[:, :], start=True, stop=True)
                for n in range(C)][-1])
            free["o_diag"] = mm
            st["attn", b] = free["bank", bank] = act.put([mm], lambda e: e.activation(
                attn_t[:, :, b * LQ:(b + 1) * LQ], blocks(ot, LQ), ACT.Identity))

        w_in = [sb(stage_b, f"w_in{i}", [P, D]) for i in range(2)]
        w_q4 = sb(stage_b, "w_q4", [P, D])
        w_hi = sb(stage_b, "w_hi", [P, C, P], F32R)
        w_lo = sb(stage_b, "w_lo", [P, C, P], F32R)
        w_quant = Quantiser(stage_b, "wq4", D)
        w_load = [stream(f"w_landed{i}") for i in range(2)]
        w_out_sem = stream("w_spilled")
        jobs = [("gu", g, r, 0, D) for g in range(2) for r in range(CI)] + \
               [("dn", 0, r, c, min(D, INNER - c)) for r in range(C) for c in range(0, INNER, D)]

        def load_weight(n):
            kind, g, r, c0, width = jobs[n]
            src = a[("w_gate", "w_up")[g]][r * P:(r + 1) * P, :] if kind == "gu" else a["w_down"][r * P:(r + 1) * P, c0:c0 + width]
            i = n % 2
            st["w", n] = sp.dma([a_done, free.get(("w_in", i))], [lambda e: copy_bits(e, w_in[i][:, 0:width], src)], w_load[i])

        def quantise_weight(n):
            kind, g, r, c0, width = jobs[n]
            i, k = n % 2, width // P
            q = w_quant.run(w_in[i][:, 0:width], w_q4[:, 0:width], width, [st["w", n]], free_q=free.get("w_q4"))
            free["w_in", i] = q
            bank, bank_read = next_bank()
            tr = pe.put([q, bank_read], lambda e: [e.transpose(
                psum[:, bank, m * P:(m + 1) * P], w_q4[:, m * P:(m + 1) * P], ident[:, :]) for m in range(k)][-1])
            free["w_q4"] = tr
            ps = psum[:, bank, 0:width].rearrange("p (m n) -> p m n", n=P)
            hi, lo = split(ps, w_hi[:, 0:k, :], w_lo[:, 0:k, :], [tr, free.get("w_hl")])
            free["bank", bank] = lo
            if kind == "gu":
                dst = [wgu_spill[g, part, :, :, r * P:(r + 1) * P] for part in range(2)]
            else:
                dst = [wdn_spill[part, :, c0 // P:c0 // P + k, r * P:(r + 1) * P] for part in range(2)]
            free["w_hl"] = st["w_spilled"] = sp.dma([hi, lo], [
                lambda e, s=s, d=d: copy_bits(e, d, s[:, 0:k, :]) for s, d in zip((w_hi, w_lo), dst)], w_out_sem)

        load_batch(0)
        load_batch(1)
        load_pack(0)
        load_weight(0)
        load_weight(1)
        normalise(0)
        for c in range(C):
            transpose_z(0, c)
        todo = list(range(len(jobs)))

        def background():
            if todo:
                n = todo.pop(0)
                quantise_weight(n)
                if n + 2 < len(jobs):
                    load_weight(n + 2)

        for b in range(NB + 1):
            cur, old, nxt = b < NB, b >= 1, b + 1 < NB
            if cur and b >= 1:
                load_pack(b)
            for slot in range(8):
                if old and 2 <= slot < 6:
                    transpose_p(b - 1, slot - 2)
                if old and slot < 4:
                    scores(b - 1, slot)
                if old and 3 <= slot < 7:
                    weigh_v(b - 1, slot - 3)
                if nxt and slot == 1:
                    normalise(b + 1)
                if nxt and 3 <= slot < 7:
                    transpose_z(b + 1, slot - 3)
                if cur and slot < 4:
                    project_k(b, slot)
                if cur and slot >= 4:
                    project_v(b, slot - 4)
                if slot in (0, 7) or (slot == 2 and b < 3):
                    background()
            if old:
                turn_o(b - 1)
            if b + 2 < NB:
                load_batch(b + 2)
        while todo:
            background()
        b_done = [st["attn", NB - 1], st["w_spilled"], (pe.sem, pe.count), (act.sem, act.count),
                  (dve.sem, dve.count), (pool.sem, pool.count)]
        stage_b.close()

        x3 = sb(ctx, "x3", [P, NT, D])
        stage_d = ExitStack()
        g_o = sb(stage_d, "g_o", [P, D])
        b_o = sb(stage_d, "b_o", [P, D])
        dw_raw = sb(stage_d, "d_wraw", [P, C, D])
        wo_hi, wo_lo, wqd_hi, wqd_lo, wkd_hi, wkd_lo, wvd_hi, wvd_lo = (
            sb(stage_d, "d_" + n, [P, C, D], F32R) for n in ("wo_hi", "wo_lo", "wq_hi", "wq_lo", "wk_hi", "wk_lo", "wv_hi", "wv_lo"))
        y = sb(stage_d, "y", [P, D])
        act_hi = sb(stage_d, "act_hi", [P, C, HALF], F32R)
        act_lo = sb(stage_d, "act_lo", [P, C, HALF], F32R)
        qk = sb(stage_d, "qk", [P, 2, C, HALF])
        raw = sb(stage_d, "qk_raw", [P, HALF])
        by_cos = sb(stage_d, "by_cos", [P, HALF])
        by_sin = sb(stage_d, "by_sin", [P, HALF])
        v_d = sb(stage_d, "v_d", [P, 4, D])
        e_sb = sb(stage_d, "e_sb", [P, 2 * H, LQ])
        a_diag = sb(stage_d, "a_diag", [P, H, P])
        a_t = sb(stage_d, "a_t", [P, H, P])
        o_sb = sb(stage_d, "o_sb", [P, D])
        cosin = sb(stage_d, "cosin", [P, 2, LQ])
        rope_swap = sb(stage_d, "rope_swap", [P, P])
        lnwb = sb(stage_d, "lnwb", [P, 2, DH])
        lams = sb(stage_d, "lams", [P, 4, DD])
        lam = sb(stage_d, "lam", [P, 8])
        mx16 = sb(stage_d, "mx16", [P, 2 * H])
        sm16 = sb(stage_d, "sm16", [P, 2 * H])
        ms8 = sb(stage_d, "ms8", [P, 2, H])
        small_d = ln_small(stage_d, "d", 1)
        d_load = [stream(f"d_landed{i}") for i in range(6)]
        d_const = sp.dma([b_done], [
            lambda e: copy_bits(e, g_o[:, :], a["g_o"].partition_broadcast(P)),
            lambda e: copy_bits(e, b_o[:, :], a["b_o"].partition_broadcast(P)),
            lambda e: copy_bits(e, cosin[:, :, :], a["cosin"]),
            lambda e: copy_bits(e, rope_swap[:, :], a["rope_swap"]),
            lambda e: copy_bits(e, lnwb[:, 0, :], a["ln_w"].partition_broadcast(P)),
            lambda e: copy_bits(e, lnwb[:, 1, :], a["ln_b"].partition_broadcast(P)),
        ] + [lambda e, k=k, n=n: copy_bits(e, lams[:, k, :], a[n].partition_broadcast(P))
             for k, n in enumerate(("lq1", "lk1", "lq2", "lk2"))] + [
            lambda e: copy_bits(e, x3[:, :, :], a["x"].rearrange("(t p) d -> p t d", p=P)),
        ], d_load[0])
        w_tok = None
        w_ready = {}
        for k, (name, hi, lo) in enumerate((("w_out", wo_hi, wo_lo), ("Wq_t", wqd_hi, wqd_lo),
                                            ("Wk_t", wkd_hi, wkd_lo), ("Wv_t", wvd_hi, wvd_lo))):
            landed = sp.dma([b_done, w_tok], [lambda e, name=name: copy_bits(e, 
                dw_raw[:, :, :], a[name].rearrange("(c p) n -> p c n", p=P))], d_load[1 + k])
            w_tok = w_ready[name] = split(dw_raw[:, :, :], hi[:, :, :], lo[:, :, :], [b_done, landed])
        s = [dve.put([d_const], lambda e, k=k: e.tensor_tensor_reduce(
            lams[:, 2 * k, :], lams[:, 2 * k, :], lams[:, 2 * k + 1, :], 1.0, 0.0, ALU.mult, ALU.add, lam[:, k:k + 1])) for k in range(2)]
        s = act.put([s], lambda e: e.activation(lam[:, 2:4], lam[:, 0:2], ACT.Exp))
        s = dve.put([s], lambda e: e.tensor_tensor(lam[:, 4:5], lam[:, 2:3], lam[:, 3:4], ALU.subtract))
        lam_ready = dve.put([s], lambda e: e.tensor_scalar(lam[:, 5:6], lam[:, 4:5], LAMBDA_INIT, None, ALU.add))
        lnw_ready = dve.put([d_const], lambda e: e.tensor_scalar(lnwb[:, :, :], lnwb[:, :, :], 1.0 - LAMBDA_INIT, None, ALU.mult))
        a_zero = dve.put([b_done], lambda e: e.memset(a_diag[:, :, :], 0.0))

        ready = {}
        last = [b_done]
        bk = {n: None for n in range(8)}

        def turn_split(t, src_tokens, src, k, reads):
            tr = pe.put([src_tokens, bk[0]], lambda e: [e.transpose(
                psum[:, 0, c * P:(c + 1) * P], src[:, c * P:(c + 1) * P], ident[:, :]) for c in range(C)][-1])
            ks = slice(k * P, (k + 1) * P)
            ps = psum[:, 0, :].rearrange("p (c n) -> p c n", c=C)
            hi, lo = split(ps, act_hi[:, :, ks], act_lo[:, :, ks], [tr, reads])
            bk[0] = lo
            return tr, [hi, lo]

        y_free = None
        free_small = None
        reads = []
        for half in range(2):
            hs = slice(half * HALF, (half + 1) * HALF)
            sp_hl = split(attn_t[:, :, hs], act_hi[:, :, :], act_lo[:, :, :], [b_done, reads])
            outs = []
            mms = []
            for k in range(4):
                t, bank, ts = 4 * half + k, 1 + k % 2, slice(k * P, (k + 1) * P)
                mm = pe.put([sp_hl, w_ready["w_out"], bk[bank]], lambda e, bank=bank, ts=ts: mm3(
                    e, psum[:, bank, :], lambda c: (act_hi[:, c, ts], act_lo[:, c, ts]),
                    lambda c: (wo_hi[:, c, :], wo_lo[:, c, :]), range(C)))
                mms.append(mm)
                ln = layernorm(lambda i, bank=bank: psum[:, bank, :], lambda i: y[:, :], 1, small_d, [mm],
                               free_small=[free_small, y_free])
                free_small = ln
                bk[bank] = ln
                m = dve.put([ln, d_const], lambda e: e.tensor_tensor(y[:, :], y[:, :], g_o[:, :], ALU.mult))
                m = dve.put([m], lambda e: e.tensor_tensor(y[:, :], y[:, :], b_o[:, :], ALU.add))
                m = dve.put([m], lambda e, t=t: e.tensor_tensor(x3[:, t, :], x3[:, t, :], y[:, :], ALU.add))
                y_free = m
                ready["x2", t] = m
            reads = mms
            tr_ok = []
            for k in range(4):
                t = 4 * half + k
                ln = layernorm(lambda i, t=t: x3[:, t, :], lambda i: y[:, :], 1, small_d, [ready["x2", t]],
                               free_small=[free_small, y_free])
                free_small = ln
                tr, hl = turn_split(t, ln, y, k, reads)
                y_free = tr
                tr_ok.append(hl)
            reads = []
            raw_free = None
            rope = []
            for which, (wh, wl, wn) in enumerate(((wqd_hi, wqd_lo, "Wq_t"), (wkd_hi, wkd_lo, "Wk_t"))):
                for n in range(C):
                    cs, bank = slice(n * P, (n + 1) * P), 1 + n % 2
                    mm = pe.put([tr_ok, w_ready[wn], bk[bank]], lambda e, bank=bank, cs=cs, wh=wh, wl=wl: mm3(
                        e, psum[:, bank, :], lambda c: (wh[:, c, cs], wl[:, c, cs]),
                        lambda c: (act_hi[:, c, :], act_lo[:, c, :]), range(C)))
                    reads.append(mm)
                    cp = act.put([mm, raw_free], lambda e, bank=bank: e.activation(raw[:, :], psum[:, bank, :], ACT.Identity))
                    bk[bank] = cp
                    sw = pe.put([cp, d_const, bk[3]], lambda e: e.matmul(
                        psum[:, 3, :], rope_swap[:, :], raw[:, :], start=True, stop=True))
                    wide = lambda k: cosin[:, k:k + 1, :].to_broadcast([P, HALF // LQ, LQ])
                    c1 = dve.put([cp, rope[-1] if rope else None], lambda e, wide=wide: e.tensor_tensor(
                        blocks(by_cos[:, :], LQ), blocks(raw[:, :], LQ), wide(0), ALU.mult))
                    c2 = dve.put([sw], lambda e, wide=wide: e.tensor_tensor(
                        blocks(by_sin[:, :], LQ), blocks(psum[:, 3, :], LQ), wide(1), ALU.mult))
                    bk[3] = c2
                    raw_free = [c1, sw]
                    rope.append(dve.put([c1, c2, ready.get(("scored", half - 1))], lambda e, which=which, n=n: e.tensor_tensor(
                        qk[:, which, n, :], by_cos[:, :], by_sin[:, :], ALU.add)))
            v_ok = []
            for k in range(4):
                bank, ts = 1 + k % 2, slice(k * P, (k + 1) * P)
                mm = pe.put([tr_ok, w_ready["Wv_t"], bk[bank]], lambda e, bank=bank, ts=ts: mm3(
                    e, psum[:, bank, :], lambda c: (act_hi[:, c, ts], act_lo[:, c, ts]),
                    lambda c: (wvd_hi[:, c, :], wvd_lo[:, c, :]), range(C)))
                reads.append(mm)
                cp = act.put([mm, ready.get(("weighed", half - 1))], lambda e, bank=bank, k=k: e.activation(v_d[:, k, :], psum[:, bank, :], ACT.Identity))
                bk[bank] = cp
                v_ok.append(cp)
            o_ready = []
            for k in range(4):
                t = 4 * half + k

                def issue(e, k=k):
                    for bb in range(2):
                        tok = slice(k * P + bb * LQ, k * P + (bb + 1) * LQ)
                        for n in range(C):
                            for j in range(4):
                                r = slice(32 * j, 32 * j + 32)
                                m = e.matmul(psum[64 * bb:64 * bb + 64, 4 + j, n * LQ:(n + 1) * LQ],
                                             qk[r, 0, n, tok], qk[r, 1, n, tok], start=True, stop=True)
                    return m
                mm = pe.put([rope, [bk[4 + j] for j in range(4)]], issue)
                ready["scored", half] = mm
                s_ps = psum[:, 4:8, 0:C * LQ].rearrange("p j (n k) -> p j n k", k=LQ)
                e_ord = e_sb[:, :, :].rearrange("p (j n) k -> p j n k", j=4)
                m1 = dve.put([mm, ready.get("mx_free")], lambda e: e.tensor_reduce(
                    mx16[:, :].rearrange("p (j n) -> p j n", j=4), s_ps, AX.X, ALU.max))
                subs = []
                for j in range(4):
                    subs.append(dve.put([m1, ready.get("e_free")], lambda e, j=j: e.tensor_tensor(
                        e_sb[:, 4 * j:4 * j + 4, :], blocks(psum[:, 4 + j, 0:C * LQ], LQ),
                        over(mx16[:, 4 * j:4 * j + 4], LQ), ALU.subtract)))
                    bk[4 + j] = subs[-1]
                ex = act.put([subs], lambda e: e.activation(e_sb[:, :, :], e_sb[:, :, :], ACT.Exp, scale=SCORE_SCALE))
                m = dve.put([ex], lambda e: e.tensor_reduce(sm16[:, :], e_sb[:, :, :], AX.X, ALU.add))
                m = dve.put([m], lambda e: e.reciprocal(sm16[:, :], sm16[:, :]))
                ml = [dve.put([m, lam_ready], lambda e, j=j: e.tensor_scalar(
                    sm16[:, 4 * j:4 * j + 4], sm16[:, 4 * j:4 * j + 4], lam[:, 5:6], None, ALU.mult)) for j in (1, 3)]
                m = dve.put([ml], lambda e: e.tensor_tensor(e_sb[:, :, :], e_sb[:, :, :], over(sm16[:, :], LQ), ALU.mult))
                ready["mx_free"] = m
                ads = []
                for par in range(2):
                    for rr in (slice(0, 64), slice(64, 128)):
                        ads.append(dve.put([m, a_zero, ready.get("a_free")], lambda e, par=par, rr=rr: e.tensor_tensor(
                            a_diag[rr, par:H:2, rr], e_sb[rr, 8 * par:8 * par + 4, :],
                            e_sb[rr, 8 * par + 4:8 * par + 8, :], ALU.subtract)))
                ready["e_free"] = ads
                ats = []
                for g in range(2):
                    tr = pe.put([ads, bk[1 + g]], lambda e, g=g: [e.transpose(
                        psum[:, 1 + g, h * P:(h + 1) * P], a_diag[:, 4 * g + h, :], ident[:, :]) for h in range(4)][-1])
                    cp = act.put([tr, ready.get("at_free")], lambda e, g=g: e.activation(
                        a_t[:, 4 * g:4 * g + 4, :], psum[:, 1 + g, :].rearrange("p (h n) -> p h n", h=4), ACT.Identity))
                    bk[1 + g] = cp
                    ats.append(cp)
                ready["a_free"] = tr
                mm = pe.put([ats, v_ok[k], bk[3]], lambda e, k=k: [e.matmul(
                    psum[:, 3, h * DH:(h + 1) * DH], a_t[:, h, :], v_d[:, k, h * DH:(h + 1) * DH],
                    start=True, stop=True) for h in range(H)][-1])
                ready["at_free"] = ready["weighed", half] = mm
                o1 = act.put([mm, y_free], lambda e: e.activation(y[:, :], psum[:, 3, :], ACT.Square))
                m = dve.put([o1, ready.get("ms_free")], lambda e: e.tensor_reduce(ms8[:, 0, :], blocks(y[:, :], DH), AX.X, ALU.add))
                m = dve.put([m], lambda e: e.tensor_scalar(ms8[:, 0, :], ms8[:, 0, :], 1.0 / DH, EPS_RMS, ALU.mult, ALU.add))
                m = pool.put([m, pow_set], lambda e: e.tensor_tensor(ms8[:, 1, :], ms8[:, 0, :], half_pow[:, 0:H], ALU.pow))
                m = dve.put([m, ready.get("o_free")], lambda e: e.tensor_tensor(
                    blocks(o_sb[:, :], DH), blocks(psum[:, 3, :], DH), over(ms8[:, 1, :], DH), ALU.mult))
                bk[3] = y_free = ready["ms_free"] = m
                for w, op in ((0, ALU.mult), (1, ALU.add)):
                    m = dve.put([m, lnw_ready], lambda e, w=w, op=op: e.tensor_tensor(
                        blocks(o_sb[:, :], DH), blocks(o_sb[:, :], DH),
                        lnwb[:, w:w + 1, :].to_broadcast([P, H, DH]), op))
                tr, hl = turn_split(t, m, o_sb, k, reads)
                ready["o_free"] = tr
                o_ready.append(hl)
            reads = []
            if half == 0:
                landed = sp.dma([mms, w_tok], [lambda e: copy_bits(e, 
                    dw_raw[:, :, :], a["Wo_t"].rearrange("(c p) n -> p c n", p=P))], d_load[5])
                wo2_hi, wo2_lo = (sb(stage_d, "d_" + n, [P, C, D], F32R) for n in ("wo2_hi", "wo2_lo"))
                wo2 = split(dw_raw[:, :, :], wo2_hi[:, :, :], wo2_lo[:, :, :], [landed, b_done])
            for k in range(4):
                t, bank, ts = 4 * half + k, 1 + k % 2, slice(k * P, (k + 1) * P)
                mm = pe.put([o_ready[k], wo2, bk[bank]], lambda e, bank=bank, ts=ts: mm3(
                    e, psum[:, bank, :], lambda c: (act_hi[:, c, ts], act_lo[:, c, ts]),
                    lambda c: (wo2_hi[:, c, :], wo2_lo[:, c, :]), range(C)))
                reads.append(mm)
                bk[bank] = ready["x3", t] = dve.put([mm], lambda e, bank=bank, t=t: e.tensor_tensor(
                    x3[:, t, :], psum[:, bank, :], x3[:, t, :], ALU.add))
        stage_d.close()
        d_done = [(q.sem, q.count) for q in (pe, act, dve, pool)]

        stage_e = ExitStack()
        wgu = [[sb(stage_e, f"wgu{g}{part}", [P, C, INNER], F32R) for part in range(2)] for g in range(2)]
        e_load = [stream(f"e_landed{i}") for i in range(2)]
        gu_ready = sp.dma([d_done, st["w_spilled"]], [lambda e, g=g, part=part: copy_bits(e, 
            wgu[g][part][:, :, :], wgu_spill[g, part]) for g in range(2) for part in range(2)], e_load[0])
        wdn = [sb(stage_e, f"wdn{part}", [P, CI, D], F32R) for part in range(2)]
        dn_ready = sp.dma([], [lambda e, part=part: copy_bits(e, 
            wdn[part][:, :, :], wdn_spill[part]) for part in range(2)], e_load[1])
        zq = sb(stage_e, "zq", [P, D])
        z2_hi = sb(stage_e, "z2_hi", [P, C, P], F32R)
        z2_lo = sb(stage_e, "z2_lo", [P, C, P], F32R)
        gate = sb(stage_e, "gate", [P, D])
        hid = sb(stage_e, "hid", [P, D])
        hid_q = sb(stage_e, "hid_q", [P, D])
        h_hi = sb(stage_e, "h_hi", [P, CI, P], F32R)
        h_lo = sb(stage_e, "h_lo", [P, CI, P], F32R)
        quant = Quantiser(stage_e, "eq", D)
        small_e = ln_small(stage_e, "e", 1)
        bk = {n: d_done for n in range(8)}
        fr = {}
        final = []
        out_sem = stream("out_stored")
        pieces = [(c0, min(D, INNER - c0)) for c0 in range(0, INNER, D)]
        for t in range(NT):
            ln = layernorm(lambda i, t=t: x3[:, t, :], lambda i: zq[:, :], 1, small_e, [d_done], free_small=[fr.get("small"), fr.get("zq")])
            fr["small"] = ln
            q = quant.run(zq[:, :], zq[:, :], D, [ln])
            tr = pe.put([q, bk[0]], lambda e: [e.transpose(
                psum[:, 0, c * P:(c + 1) * P], zq[:, c * P:(c + 1) * P], ident[:, :]) for c in range(C)][-1])
            fr["zq"] = tr
            zs = split(psum[:, 0, :].rearrange("p (c n) -> p c n", c=C), z2_hi[:, :, :], z2_lo[:, :, :], [tr, fr.get("z2")])
            bk[0] = zs[1]
            hs_ready = []
            for m, (c0, w) in enumerate(pieces):
                mms = []
                for g in range(2):
                    bank = 1 + (2 * m + g) % 4
                    mms.append(pe.put([zs, gu_ready, bk[bank]], lambda e, g=g, bank=bank, c0=c0, w=w: mm3(
                        e, psum[:, bank, 0:w], lambda c: (z2_hi[:, c, :], z2_lo[:, c, :]),
                        lambda c: (wgu[g][0][:, c, c0:c0 + w], wgu[g][1][:, c, c0:c0 + w]), range(C))))
                gb, ub = 1 + (2 * m) % 4, 1 + (2 * m + 1) % 4
                fr["z2"] = mms[-1]
                sl = act.put([mms[0], fr.get("gate"), d_done], lambda e, gb=gb, w=w: e.activation(gate[:, 0:w], psum[:, gb, 0:w], ACT.Silu))
                bk[gb] = sl
                hm = dve.put([sl, mms[1], fr.get("hid")], lambda e, ub=ub, w=w: e.tensor_tensor(
                    hid[:, 0:w], psum[:, ub, 0:w], gate[:, 0:w], ALU.mult))
                bk[ub] = fr["gate"] = hm
                q = quant.run(hid[:, 0:w], hid_q[:, 0:w], w, [hm], free_q=fr.get("hid_q"))
                fr["hid"] = q
                n = w // P
                tr = pe.put([q, bk[5 + m % 2]], lambda e, n=n, m=m: [e.transpose(
                    psum[:, 5 + m % 2, i * P:(i + 1) * P], hid_q[:, i * P:(i + 1) * P], ident[:, :]) for i in range(n)][-1])
                fr["hid_q"] = tr
                s = split(psum[:, 5 + m % 2, 0:w].rearrange("p (c n) -> p c n", n=P), h_hi[:, c0 // P:c0 // P + n, :],
                          h_lo[:, c0 // P:c0 // P + n, :], [tr, fr.get("h_t")])
                bk[5 + m % 2] = s[1]
                hs_ready.append(s)
            mm = pe.put([hs_ready, dn_ready, bk[7]], lambda e: mm3(
                e, psum[:, 7, :], lambda c: (h_hi[:, c, :], h_lo[:, c, :]),
                lambda c: (wdn[0][:, c, :], wdn[1][:, c, :]), range(CI)))
            fr["h_t"] = mm
            bk[7] = fin = dve.put([mm], lambda e, t=t: e.tensor_tensor(x3[:, t, :], psum[:, 7, :], x3[:, t, :], ALU.add))
            final = sp.dma([fin], [lambda e, t=t: copy_bits(e, out[t * P:(t + 1) * P, :], x3[:, t, :])], out_sem)
        stage_e.close()

        block = ctx.enter_context(nc.Block())

        @block.tensor
        def _(e):
            pe.emit(e)

        @block.vector
        def _(e):
            dve.emit(e)

        @block.scalar
        def _(e):
            act.emit(e)

        @block.gpsimd
        def _(e):
            pool.emit(e)

        @block.sync
        def _(e):
            sp.emit(e)
            e.wait_ge(final[0], final[1])


def constants():
    inv = (1.0 / np.float32(10000.0) ** (np.arange(0, DD, 2, dtype=np.float32) / np.float32(DD))).astype(np.float32)
    freq = np.arange(LQ, dtype=np.float32)[:, None] * inv[None, :]
    freq = np.repeat(freq, 2, axis=-1)
    table = np.stack([np.cos(freq), np.sin(freq)]).astype(np.float32)
    cosin = np.ascontiguousarray(np.tile(table.transpose(2, 0, 1), (P // DD, 1, 1)))
    swap = np.zeros((P, P), np.float32)
    for i in range(0, P, 2):
        swap[i + 1, i] = -1.0
        swap[i, i + 1] = 1.0
    eye = np.eye(P, dtype=np.float32)
    return {"ident": eye, "stacked": np.ascontiguousarray(np.concatenate([eye[:LQ, :LQ]] * 2)),
            "cosin": cosin, "rope_swap": swap}


def kernel(**inputs):
    import concourse.bacc as bacc
    from concourse.bass_utils import run_bass_kernel_spmd

    f = {k: np.asarray(v) for k, v in inputs.items()}
    arrays = constants()
    arrays["x"] = f["x"].reshape(T, D)
    arrays["ctx"] = f["ctx_1024"]
    arrays["mask"] = f["mask_BxS2_bf1"].reshape(NB, P, CS).transpose(0, 2, 1).reshape(NB, S).view(np.uint8)
    arrays["cols"] = np.stack([f["L0_xattn_" + n].reshape(C, P).T for n in ("g_x", "b_x", "g_l", "b_l")], axis=1)
    for name in ("w_q", "w_kv", "w_out", "g_o", "b_o"):
        arrays[name] = f["L0_xattn_" + name]
    for name in ("Wq", "Wk", "Wv", "Wo"):
        arrays[name + "_t"] = f["L0_attn_" + name].T
    for short, name in (("lq1", "lambda_q1"), ("lk1", "lambda_k1"), ("lq2", "lambda_q2"), ("lk2", "lambda_k2"),
                        ("ln_w", "ln_w"), ("ln_b", "ln_b")):
        arrays[short] = f["L0_attn_" + name]
    for name in ("w_gate", "w_up", "w_down"):
        arrays[name] = f["L0_ffn_" + name]
    arrays = {k: np.ascontiguousarray(v) for k, v in arrays.items()}

    nc = bacc.Bacc("TRN2", target_bir_lowering=False, num_devices=1)
    aps = {k: nc.dram_tensor("in_" + k, v.shape, mybir.dt.from_np(v.dtype), kind="ExternalInput").ap()
           for k, v in arrays.items()}
    out = nc.dram_tensor("out", (T, D), F32, kind="ExternalOutput").ap()
    perceiver(nc, aps, out)
    r = run_bass_kernel_spmd(nc, [{"in_" + k: v for k, v in arrays.items()}], core_ids=[0])
    return r.results[0]["out"].reshape(NB, LQ, D)
```
